# Optimizing a Trainium2 kernel written in Bass

```python
import numpy as np
import jax
import jax.numpy as jnp

def _softmax(x, axis=-1):
    return jax.nn.softmax(x, axis=axis)

def _gelu(x):
    return jax.nn.gelu(x, approximate=True)

def _silu(x):
    return jax.nn.silu(x)

def _sigmoid(x):
    return jax.nn.sigmoid(x)

def _layernorm(x, axis=-1, eps=1e-05):
    m = jnp.mean(x, axis=axis, keepdims=True)
    v = jnp.var(x, axis=axis, keepdims=True)
    return (x - m) / jnp.sqrt(v + eps)

def _scatter_add(tgt, idx, src, axis=0):
    return tgt.at[idx].add(src)

def _segment_sum(src, seg, n):
    return jax.ops.segment_sum(src, seg, n)
kernel_name = 'mk_gnn_preln_d2_gnn_r8_839f94'

def setup_inputs(seed: int=0):
    np.random.seed(seed)
    _w = jnp.asarray

    def _rec_inputs():
        import jax
        import jax.numpy as jnp
        _gk = jax.random.key(seed)
        x = -0.0001006 + 1 * jax.random.normal(jax.random.fold_in(_gk, 1), (12500, 96), jnp.float32)
        _s = jax.random.randint(jax.random.fold_in(_gk, 2), (200000,), 0, 12500, jnp.int32)
        _d = jax.random.randint(jax.random.fold_in(_gk, 3), (200000,), 0, 12500, jnp.int32)
        _loop = jnp.arange(12500, dtype=jnp.int32)
        src = jnp.concatenate([_s, _d, _loop])
        dst = jnp.concatenate([_d, _s, _loop])
        _o = jnp.argsort(dst, stable=True)
        src = src[_o]
        dst = dst[_o]
        edge_attr_17 = jax.random.uniform(jax.random.fold_in(_gk, 11), (412500, 17), jnp.float32, 0.0, 1)
        edge_attr_32 = 0.000196303 + 1.00016 * jax.random.normal(jax.random.fold_in(_gk, 12), (412500, 32), jnp.float32)
        return (x, src, dst, edge_attr_17, edge_attr_32)
    x, src, dst, edge_attr_17, edge_attr_32 = _rec_inputs()

    def _L0_gnn_setup():
        import jax, jax.numpy as jnp
        import numpy as np
        N, E = (6250, 100000)
        DIN = DOUT = 96
        DE = 32

        def _egnn_conv(x, src, dst, edge_attr, W_msg, W_edge, W_root, b):
            msg = x[src] @ W_msg + edge_attr @ W_edge
            agg = jax.ops.segment_max(msg, dst, num_segments=x.shape[0])
            agg = jnp.where(jnp.isneginf(agg), 0.0, agg)
            return agg + x @ W_root + b
        key = jax.random.key(seed)
        ks = jax.random.split(key, 10)
        rn = lambda k, sh, sc: jax.random.normal(k, sh, jnp.float32) * sc
        return {'X': rn(ks[0], (N, DIN), 1.0), 'edge_index': jax.random.randint(ks[1], (2, E), 0, N, jnp.int32), 'edge_attr': rn(ks[2], (E, DE), 1.0), 'W1_msg': rn(ks[3], (DIN, DOUT), DIN ** (-0.5)), 'W1_edge': rn(ks[4], (DE, DOUT), DE ** (-0.5)), 'W1_root': rn(ks[5], (DIN, DOUT), DIN ** (-0.5)), 'b1': jnp.zeros((DOUT,), jnp.float32), 'W2_msg': rn(ks[6], (DOUT, DOUT), DOUT ** (-0.5)), 'W2_edge': rn(ks[7], (DE, DOUT), DE ** (-0.5)), 'W2_root': rn(ks[8], (DOUT, DOUT), DOUT ** (-0.5)), 'b2': jnp.zeros((DOUT,), jnp.float32)}
    _L0_gnn_all = _L0_gnn_setup()
    _L0_gnn_in = {k: v for k, v in _L0_gnn_all.items() if k in ('W1_msg', 'W1_edge', 'W1_root', 'b1', 'W2_msg', 'W2_edge', 'W2_root', 'b2')}
    del _L0_gnn_all

    def _L1_gnn_setup():
        import jax, jax.numpy as jnp
        import numpy as np
        N = 6250
        E = 100000
        D = 96
        ED = 17
        key = jax.random.key(seed)
        ks = jax.random.split(key, 12)
        x = jax.random.normal(ks[0], (N, D), dtype=jnp.float32)
        edge_index = jax.random.randint(ks[1], (2, E), 0, N, dtype=jnp.int64)
        edge_attr = jax.random.uniform(ks[2], (E, ED), dtype=jnp.float32)
        s = 1.0 / np.sqrt(ED)
        W1 = jax.random.uniform(ks[3], (D, ED), jnp.float32, -s, s)
        b1 = jax.random.uniform(ks[4], (D,), jnp.float32, -s, s)
        s = 1.0 / np.sqrt(D)
        W2 = jax.random.uniform(ks[5], (D, D), jnp.float32, -s, s)
        b2 = jax.random.uniform(ks[6], (D,), jnp.float32, -s, s)
        Ws = jax.random.uniform(ks[7], (D, D), jnp.float32, -s, s)
        bs = jax.random.uniform(ks[8], (D,), jnp.float32, -s, s)
        Wn = jax.random.uniform(ks[9], (D, D), jnp.float32, -s, s)
        bn = jax.random.uniform(ks[10], (D,), jnp.float32, -s, s)
        return {'x': x, 'edge_index': edge_index, 'edge_attr': edge_attr, 'W1': W1, 'b1': b1, 'W2': W2, 'b2': b2, 'Ws': Ws, 'bs': bs, 'Wn': Wn, 'bn': bn}
    _L1_gnn_all = _L1_gnn_setup()
    _L1_gnn_in = {k: v for k, v in _L1_gnn_all.items() if k in ('W1', 'b1', 'W2', 'b2', 'Ws', 'bs', 'Wn', 'bn')}
    del _L1_gnn_all
    return {'x': x, 'src': src, 'dst': dst, 'edge_attr_17': edge_attr_17, 'edge_attr_32': edge_attr_32, 'L0_gnn_W1_msg': _L0_gnn_in['W1_msg'], 'L0_gnn_W1_edge': _L0_gnn_in['W1_edge'], 'L0_gnn_W1_root': _L0_gnn_in['W1_root'], 'L0_gnn_b1': _L0_gnn_in['b1'], 'L0_gnn_W2_msg': _L0_gnn_in['W2_msg'], 'L0_gnn_W2_edge': _L0_gnn_in['W2_edge'], 'L0_gnn_W2_root': _L0_gnn_in['W2_root'], 'L0_gnn_b2': _L0_gnn_in['b2'], 'L1_gnn_W1': _L1_gnn_in['W1'], 'L1_gnn_b1': _L1_gnn_in['b1'], 'L1_gnn_W2': _L1_gnn_in['W2'], 'L1_gnn_b2': _L1_gnn_in['b2'], 'L1_gnn_Ws': _L1_gnn_in['Ws'], 'L1_gnn_bs': _L1_gnn_in['bs'], 'L1_gnn_Wn': _L1_gnn_in['Wn'], 'L1_gnn_bn': _L1_gnn_in['bn']}

def reference(x, src, dst, edge_attr_17, edge_attr_32, L0_gnn_W1_msg, L0_gnn_W1_edge, L0_gnn_W1_root, L0_gnn_b1, L0_gnn_W2_msg, L0_gnn_W2_edge, L0_gnn_W2_root, L0_gnn_b2, L1_gnn_W1, L1_gnn_b1, L1_gnn_W2, L1_gnn_b2, L1_gnn_Ws, L1_gnn_bs, L1_gnn_Wn, L1_gnn_bn):
    import jax
    import jax.numpy as jnp

    def _L0_gnn_ref(X, edge_index, edge_attr, W1_msg, W1_edge, W1_root, b1, W2_msg, W2_edge, W2_root, b2):
        import jax, jax.numpy as jnp
        import numpy as np
        N, E = (6250, 100000)
        DIN = DOUT = 96
        DE = 32

        def _egnn_conv(x, src, dst, edge_attr, W_msg, W_edge, W_root, b):
            msg = x[src] @ W_msg + edge_attr @ W_edge
            agg = jax.ops.segment_max(msg, dst, num_segments=x.shape[0])
            agg = jnp.where(jnp.isneginf(agg), 0.0, agg)
            return agg + x @ W_root + b
        src, dst = (edge_index[0], edge_index[1])
        c1 = jax.nn.leaky_relu(_egnn_conv(X, src, dst, edge_attr, W1_msg, W1_edge, W1_root, b1))
        c2 = jax.nn.leaky_relu(_egnn_conv(c1, src, dst, edge_attr, W2_msg, W2_edge, W2_root, b2))
        return c2

    def _L1_gnn_ref(x, edge_index, edge_attr, W1, b1, W2, b2, Ws, bs, Wn, bn):
        import jax, jax.numpy as jnp
        import numpy as np
        N = 6250
        E = 100000
        D = 96
        ED = 17
        src, dst = (edge_index[0], edge_index[1])
        h = jax.nn.relu(edge_attr @ W1.T + b1)
        w = h @ W2.T + b2
        msg = w * x[src]
        agg = jax.ops.segment_sum(msg, dst, num_segments=x.shape[0])
        return jax.nn.relu(x @ Ws.T + bs + agg @ Wn.T + bn)
    edge_index = jnp.stack([src, dst])
    h = jnp.maximum(_layernorm(x, axis=-1), 0.0)
    x = x + _L0_gnn_ref(h, edge_index, edge_attr_32, L0_gnn_W1_msg, L0_gnn_W1_edge, L0_gnn_W1_root, L0_gnn_b1, L0_gnn_W2_msg, L0_gnn_W2_edge, L0_gnn_W2_root, L0_gnn_b2)
    h = jnp.maximum(_layernorm(x, axis=-1), 0.0)
    x = x + _L1_gnn_ref(h, edge_index, edge_attr_17, L1_gnn_W1, L1_gnn_b1, L1_gnn_W2, L1_gnn_b2, L1_gnn_Ws, L1_gnn_bs, L1_gnn_Wn, L1_gnn_bn)
    return x

_drawn_inputs = setup_inputs


def setup_inputs(seed=0):
    import zlib

    import numpy as np

    out = dict(_drawn_inputs(seed))
    spreads = {'L0_gnn_b1': (0.0, 0.323), 'L0_gnn_b2': (0.0, 0.481)}
    factors = {'edge_attr_17': 2.7, 'L1_gnn_bs': 6.401, 'L1_gnn_bn': 6.572}
    for name, (base, spread) in spreads.items():
        noise = np.random.default_rng([zlib.crc32(name.encode()), seed]).standard_normal(out[name].shape)
        drawn = base * np.exp(spread * noise) if base else spread * noise
        out[name] = jnp.asarray(drawn.astype(out[name].dtype))
    for name, factor in factors.items():
        out[name] = (out[name] * factor).astype(out[name].dtype)
    return out
```

```python
from contextlib import ExitStack

import concourse.bass as bass
from concourse import mybir

ALU = mybir.AluOpType
ACT = mybir.ActivationFunctionType
AX = mybir.AxisListType
F32 = mybir.dt.float32
BF16 = mybir.dt.bfloat16
I32 = mybir.dt.int32

P = 128
N, D, E = 12500, 96, 412500
DE0, DE1 = 32, 17
DE1P = 18

SB = 5
RING = 3
T = -(-E // (P * SB * RING)) * SB * RING
ITERS = T // (SB * RING)
BATCHES = ITERS * RING
BD = SB * D
ZERO_ROW = P * T

NT = -(-N // P)
NPAD = NT * P
NB = 7
NRING = 2
NITERS = NT // (NB * NRING)
NBATCHES = NITERS * NRING
HALF = 4

HI = -(-N // P)
HI_SHIFT, LO_MASK = 7, 127

EPS = 1e-5
SLOPE = 0.01
FLT_MAX = 3.4028234663852886e38
FAR = float(1 << 20)

assert NT % (NB * NRING) == 0 and NITERS > 2 and ITERS > 2


def gnn_program(nc, x, src, dst, ea32, ea17, w1_msg, w1_root, w1_edge, w2_msg, w2_root, w2_edge,
                w3_h, b3_h, w3_e, w3_self, w3_nbr, out):
    with ExitStack() as ctx:
        def sb(name, shape, dt=F32):
            return ctx.enter_context(nc.sbuf_tensor(name, shape, dt))

        def sem(name):
            return ctx.enter_context(nc.semaphore(name))

        def dram(name, shape, dt=F32):
            return nc.dram_tensor(name, shape, dt).ap()

        table = [dram(f"table{k}", [NPAD, D]) for k in range(3)]
        running = dram("running", [P * T + 1, D])
        node_row_dram = dram("node_row_dram", [HI, P], I32)

        running_v = running[0:P * T, :].rearrange("(p t) f -> p (t f)", p=P)
        table_v = [t.rearrange("(p t) f -> p (t f)", p=P) for t in table]
        node_row_v = node_row_dram.rearrange("h l -> (h l)").rearrange("(p t) -> p t", p=P)

        wt = {}
        weight_srcs = [("w1_msg", w1_msg, D), ("w1_root", w1_root, D + 1), ("w1_edge", w1_edge, DE0),
                       ("w2_msg", w2_msg, D), ("w2_root", w2_root, D + 1), ("w2_edge", w2_edge, DE0),
                       ("w3_h", w3_h, DE1P), ("w3_e", w3_e, D + 1), ("w3_self", w3_self, D + 2),
                       ("w3_nbr", w3_nbr, D)]
        for name, _, rows in weight_srcs:
            wt[name] = sb(name + "_sb", [rows, D])
        b3_sb = sb("b3_sb", [D, 1])

        resid = sb("resid", [P, NT * D])
        root = sb("root", [P, NT * D])
        keep_mul = sb("keep_mul", [P, T])
        digits = sb("digits", [P, 2, T], I32)
        dst_sb = sb("dst_sb", [P, T + 1], I32)
        slot_i = digits[:, 0, :]
        work = digits[:, 1, :].bitcast(F32)

        src_ring = sb("src_ring", [P, RING, SB], I32)
        rows_ring = sb("rows_ring", [P, RING, SB, D])
        state_ring = sb("state_ring", [P, RING, SB, D])
        attr_ring = sb("attr_ring", [DE0, RING, SB * P])
        keep_ring = sb("keep_ring", [P, RING, SB])
        digit_ring = sb("digit_ring", [P, RING, 2, SB], BF16)
        lo_hot = sb("lo_hot", [P, RING, SB, P], BF16)
        hi_hot = sb("hi_hot", [P, RING, SB, HI], BF16)
        hid_ring = sb("hid_ring", [D + 1, RING, SB * P])

        row_ring = sb("row_ring", [P, NRING, NB], I32)
        agg = sb("agg", [P, NRING, NB, D])
        act_t = sb("act_t", [P, NRING, NB, D])
        feat = sb("feat", [P, NRING, NB, D])
        feat_t = sb("feat_t", [D + 2, NRING, NB * P])
        store = sb("store", [P, NRING, NB, D])
        stats = sb("stats", [P, NB, 6])
        mean_var = sb("mean_var", [P, NB, 2])
        std = sb("std", [P, NB])
        rstd = sb("rstd", [P, NB])
        eps = sb("eps", [P, 1])
        far_below = sb("far_below", [P, 1])

        ident = sb("ident", [P, P])
        iota_i = sb("iota_i", [P, P], I32)
        iota_b = sb("iota_b", [P, P], BF16)
        first_i = sb("first_i", [P, 1], I32)
        upper = sb("upper", [P, P])
        cont_mul = sb("cont_mul", [P, 1])
        cont_add = sb("cont_add", [P, 1])
        whole = sb("whole", [P, 1])
        whole_b = sb("whole_b", [P, D])
        whole_mul = sb("whole_mul", [D, P])
        whole_add = sb("whole_add", [D, P])
        fix = sb("fix", [P, 1])
        fix_row = sb("fix_row", [P, 1], I32)
        fix_vals = sb("fix_vals", [P, D])
        ends = sb("ends", [D, P + 1])
        count = sb("count", [HI, P])
        total = sb("total", [HI, 1])
        before = sb("before", [HI, 1])
        prefix = sb("prefix", [HI, P])
        empty = sb("empty", [HI, P])
        node_row_f = sb("node_row_f", [HI, P])
        node_row_i = sb("node_row_i", [HI, P], I32)
        zeros = sb("zeros", [P, P])
        zeros_b = sb("zeros_b", [P, P], BF16)

        bank = [ctx.enter_context(nc.psum_tensor(f"bank{k}", [P, 512], F32)) for k in range(8)]
        term = bank[0:RING]
        hid_ps = bank[3:5]
        count_ps = bank[7]
        tail_ps, shift_ps, whole_ps, before_ps = bank[3], bank[4], bank[5], bank[6]
        tr_ps = bank[0:2]
        msg_ps = bank[2:4]
        root_ps = [bank[4:6], bank[6:8]]

        block = ctx.enter_context(nc.Block())

        s_weights = sem("weights_loaded")
        s_dst = sem("dst_loaded")
        s_consts = sem("pool_consts_ready")
        s_zero = sem("vector_consts_ready")
        s_ident = sem("identity_ready")
        s_masks = sem("masks_step")
        s_setup = sem("segment_layout_ready")
        s_whole_bc = sem("whole_broadcast_ready")
        s_whole_t = sem("whole_transposed")
        s_whole_m = sem("whole_masks_ready")
        s_zrow = sem("zero_row_written")
        s_hot = sem("one_hots_ready")
        s_hist = sem("one_hots_counted")
        s_hist_end = sem("histogram_complete")
        s_pref = sem("prefix_step")
        s_total = sem("totals_ready")
        s_before = sem("counts_before_ready")
        s_noderow = sem("node_rows_ready")
        s_noderow_w = sem("node_rows_written")

        LAYERS = range(3)
        src_loaded = [[sem(f"src_loaded_{k}_{r}") for r in range(RING)] for k in LAYERS]
        attr_loaded = [[sem(f"attr_loaded_{k}_{r}") for r in range(RING)] for k in LAYERS]
        gathered = [[sem(f"gathered_{k}_{r}") for r in range(RING)] for k in LAYERS]
        dumped = [[sem(f"dumped_{k}_{r}") for r in range(RING)] for k in LAYERS]
        gather_turn = sem("gather_turn")
        keep_copied = [sem(f"keep_copied_{k}") for k in LAYERS]
        term_ready = [sem(f"term_ready_{k}") for k in LAYERS]
        combined = [sem(f"messages_ready_{k}") for k in LAYERS]
        state_step = [sem(f"state_step_{k}") for k in LAYERS]
        scanned = [sem(f"batch_scanned_{k}") for k in LAYERS]
        state_init = [sem(f"state_init_{k}") for k in LAYERS]
        hid_mm = sem("hidden_product_ready")
        hid_ready = sem("hidden_ready")
        tail_t = sem("tails_transposed")
        ends_ready = sem("ends_scanned")
        ends_back = sem("ends_transposed_back")
        fix_loaded = sem("fix_rows_loaded")
        fix_ready = sem("fix_rows_ready")
        fix_stored = sem("fix_rows_stored")
        PHASES = range(4)
        rowidx_loaded = [[sem(f"node_rows_loaded_{k}_{q}") for q in range(NRING)] if k else None for k in PHASES]
        agg_loaded = [[sem(f"aggregates_loaded_{k}_{q}") for q in range(NRING)] for k in PHASES]
        agg_turn = sem("aggregate_turn")
        node_sum = {k: sem(f"node_sum_{k}") for k in (1, 2, 3)}
        node_act = {k: sem(f"node_activated_{k}") for k in (2,)}
        conv_act = sem("second_convolution_activated")
        stat_step = {k: sem(f"layernorm_step_{k}") for k in (0, 2)}
        aggr_turn = sem("layernorm_turn")
        var_ready = {k: sem(f"variance_ready_{k}") for k in (0, 2)}
        std_ready = {k: sem(f"deviation_ready_{k}") for k in (0, 2)}
        normed = {k: sem(f"normalised_{k}") for k in (0, 2)}
        feat_ready = {k: sem(f"features_ready_{k}") for k in (0, 1, 2)}
        resid_kept = {k: sem(f"residual_kept_{k}") for k in (0, 2)}
        transposed = [sem(f"features_transposed_{k}") for k in PHASES]
        feat_t_ready = [sem(f"transposed_features_ready_{k}") for k in PHASES]
        msg_done = {k: sem(f"message_products_ready_{k}") for k in (0, 1, 3)}
        root_done = {k: sem(f"root_products_ready_{k}") for k in (0, 1, 2)}
        root_kept = {k: sem(f"root_terms_kept_{k}") for k in (0, 1, 2)}
        store_ready = [sem(f"store_rows_ready_{k}") for k in PHASES]
        stored = [[sem(f"rows_stored_{k}_{q}") for q in range(NRING)] for k in PHASES]

        NW = len(weight_srcs) + 1
        MSG_W = [wt["w1_msg"], wt["w2_msg"], None, wt["w3_nbr"]]
        ROOT_W = [(wt["w1_root"], D + 1), (wt["w2_root"], D + 1), (wt["w3_self"], D + 2), None]

        def flat(ap):
            return ap.rearrange("p n f -> p (n f)")

        def tile_cols(banks, k):
            return banks[k // HALF][:, (k % HALF) * D:(k % HALF) * D + D]

        def edge_loop(eng, body):
            body(0, True)
            with eng.Fori(1, ITERS) as i:
                body(i, False)

        def node_loop(eng, body):
            body(0, True)
            with eng.Fori(1, NITERS) as i:
                body(i, False)

        def skewed_loop(eng, iters, ring, lead, follow):
            def body(i, first, last):
                for r in range(ring):
                    if r < ring - 1:
                        lead(i, r + 1, first)
                    elif not last:
                        lead(i + 1, 0, False)
                    follow(i, r, first)

            lead(0, 0, True)
            body(0, True, False)
            with eng.Fori(1, iters - 1) as i:
                body(i, False, False)
            body(iters - 1, False, True)

        def node_cols(i, q):
            return bass.ds((i * NRING + q) * (NB * D), NB * D)

        @block.sync
        def _(sp):
            sp.dma_start(dst_sb[:, :], bass.AP(tensor=dst.tensor, offset=0, ap=[[T, P], [1, T + 1]])
                         ).then_inc(s_dst, 16)

            def node_phase(k):
                def load(i, q):
                    if k == 0:
                        sp.dma_start(flat(agg[:, q]), x[:, node_cols(i, q)]).then_inc(agg_loaded[0][q], 16)
                    else:
                        sp.dma_start(row_ring[:, q, :], node_row_v[:, bass.ds((i * NRING + q) * NB, NB)]
                                     ).then_inc(rowidx_loaded[k][q], 16)

                def store_rows(i, q):
                    sp.wait_ge(feat_ready[2] if k == 2 else store_ready[k], i * NRING + q + 1)
                    dest = out[:, node_cols(i, q)] if k == 3 else table_v[k][:, node_cols(i, q)]
                    source = feat if k == 2 else store
                    sp.dma_start(dest, flat(source[:, q])).then_inc(stored[k][q], 16)

                def body(i, more):
                    for q in range(NRING):
                        if more:
                            if k == 0:
                                sp.wait_ge(normed[0], i * NRING + q + 1)
                                sp.wait_ge(resid_kept[0], i * NRING + q + 1)
                            else:
                                sp.wait_ge(agg_loaded[k][q], (i + 1) * 16 * NB)
                            load(i + 1, q)
                        store_rows(i, q)

                if k == 1:
                    sp.wait_ge(s_noderow, 1)
                    sp.dma_start(node_row_dram[:, :], node_row_i[:, :]).then_inc(s_noderow_w, 16)
                    sp.wait_ge(s_noderow_w, 16)
                for q in range(NRING):
                    load(0, q)
                if k < 3:
                    first_loads(k)
                with sp.Fori(0, NITERS - 1) as i:
                    body(i, True)
                body(NITERS - 1, False)

            def load_src(k, b, r):
                sp.dma_start(src_ring[:, r, :], src[:, bass.ds(b * SB, SB)]).then_inc(src_loaded[k][r], 16)

            def load_attr(k, b, r):
                attr, width = (ea17, DE1P) if k == 2 else (ea32, DE0)
                sp.dma_start(attr_ring[0:width, r, :], attr[:, bass.ds(b * (SB * P), SB * P)]
                             ).then_inc(attr_loaded[k][r], 16)

            def first_loads(k):
                if k > 0:
                    sp.wait_ge(term_ready[k - 1], BATCHES)
                for r in range(RING):
                    if k > 0:
                        sp.wait_ge(gathered[k - 1][r], 16 * SB * ITERS)
                    load_src(k, r, r)
                    load_attr(k, r, r)

            def edge_phase(k):
                def body(i, more):
                    for r in range(RING):
                        if more:
                            sp.wait_ge(gathered[k][r], (i + 1) * 16 * SB)
                            load_src(k, (i + 1) * RING + r, r)
                            sp.wait_ge(hid_mm if k == 2 else term_ready[k], i * RING + r + 1)
                            load_attr(k, (i + 1) * RING + r, r)
                        sp.wait_ge(scanned[k], i * RING + r + 1)
                        sp.dma_start(running_v[:, bass.ds((i * RING + r) * BD, BD)], flat(state_ring[:, r])
                                     ).then_inc(dumped[k][r], 16)

                with sp.Fori(0, ITERS - 1) as i:
                    body(i, True)
                body(ITERS - 1, False)

            sp.wait_ge(s_zero, 1)
            sp.dma_start(running[P * T:P * T + 1, :], zeros[0:1, 0:D]).then_inc(s_zrow, 16)
            node_phase(0)
            for k in LAYERS:
                edge_phase(k)
                node_phase(k + 1)
            for q in range(NRING):
                sp.wait_ge(stored[3][q], 16 * NITERS)

        @block.gpsimd
        def _(pool):
            pool.iota(iota_i[:, :], [[1, P]], base=0, channel_multiplier=0).then_inc(s_consts, 1)
            pool.iota(first_i[:, :], [[0, 1]], base=0, channel_multiplier=T).then_inc(s_consts, 1)
            pool.iota(slot_i, [[1, T]], base=0, channel_multiplier=0).then_inc(s_consts, 1)
            pool.wait_ge(s_zero, 3)
            pool.affine_select(out=ident[:, :], in_=ident[:, :], compare_op=ALU.not_equal, fill=1.0,
                               base=0, pattern=[[-1, P]], channel_multiplier=1).then_inc(s_ident, 1)
            pool.affine_select(out=upper[:, :], in_=upper[:, :], compare_op=ALU.is_gt, fill=0.0,
                               base=0, pattern=[[1, P]], channel_multiplier=-1).then_inc(s_ident, 1)

            def edge_phase(k):
                for q in range(NRING):
                    pool.wait_ge(stored[k][q], 16 * NITERS)

                def body(i, first):
                    for r in range(RING):
                        pool.wait_ge(src_loaded[k][r], (i + 1) * 16)
                        if not first:
                            pool.wait_ge(scanned[k], (i - 1) * RING + r + 1)
                        pool.sem_inc(gather_turn, 1)
                        for c in range(SB):
                            pool.indirect_dma_start(
                                rows_ring[:, r, c, :], None, table[k][:, :],
                                bass.IndirectOffsetOnAxis(ap=src_ring[:, r, c:c + 1], axis=0),
                            ).then_inc(gathered[k][r], 16)

                edge_loop(pool, body)

            def stitch(k):
                for r in range(RING):
                    pool.wait_ge(dumped[k][r], 16 * ITERS)
                if k == 0:
                    pool.wait_ge(s_setup, 1)
                pool.indirect_dma_start(fix_vals[:, :], None, running[:, :],
                                        bass.IndirectOffsetOnAxis(ap=fix_row[:, 0:1], axis=0)
                                        ).then_inc(fix_loaded, 16)
                pool.wait_ge(fix_ready, k + 1)
                pool.indirect_dma_start(running[:, :], bass.IndirectOffsetOnAxis(ap=fix_row[:, 0:1], axis=0),
                                        fix_vals[:, :], None).then_inc(fix_stored, 16)
                pool.wait_ge(fix_stored, 16 * (k + 1))
                if k == 0:
                    pool.wait_ge(s_zrow, 16)

            def node_phase(k):
                def body(i, first):
                    for q in range(NRING):
                        pool.wait_ge(rowidx_loaded[k][q], (i + 1) * 16)
                        if not first:
                            free = transposed[3] if k == 3 else node_sum[k]
                            pool.wait_ge(free, (i - 1) * NRING + q + 1)
                        pool.sem_inc(agg_turn, 1)
                        for c in range(NB):
                            pool.indirect_dma_start(
                                agg[:, q, c, :], None, running[:, :],
                                bass.IndirectOffsetOnAxis(ap=row_ring[:, q, c:c + 1], axis=0),
                            ).then_inc(agg_loaded[k][q], 16)

                node_loop(pool, body)

            for k in LAYERS:
                edge_phase(k)
                stitch(k)
                node_phase(k + 1)

        @block.tensor
        def _(pe):
            pe.wait_ge(s_weights, 16 * NW)
            pe.wait_ge(s_ident, 2)

            def transpose_batch(k, i, q, first):
                source = agg if k == 3 else feat
                if k == 3:
                    pe.wait_ge(agg_loaded[3][q], (i + 1) * 16 * NB)
                else:
                    pe.wait_ge(feat_ready[k], i * NRING + q + 1)
                if not (first and q == 0):
                    pe.wait_ge(feat_t_ready[k], i * NRING + q)
                for c in range(NB):
                    last = nc.tensor.transpose(tr_ps[c // HALF][0:D, (c % HALF) * P:(c % HALF) * P + P],
                                               source[:, q, c, :], ident[:, :])
                last.then_inc(transposed[k], 1)

            def product_batch(k, i, q, first):
                pe.wait_ge(feat_t_ready[k], i * NRING + q + 1)
                if not (first and q == 0):
                    if k in msg_done:
                        pe.wait_ge(store_ready[k], i * NRING + q)
                if k in msg_done:
                    for c in range(NB):
                        last = nc.tensor.matmul(tile_cols(msg_ps, c), feat_t[0:D, q, c * P:c * P + P],
                                                MSG_W[k][:, :], start=True, stop=True)
                    last.then_inc(msg_done[k], 1)
                if k in root_done:
                    w, rows = ROOT_W[k]
                    if not first:
                        pe.wait_ge(root_kept[k], (i - 1) * NRING + q + 1)
                    for c in range(NB):
                        last = nc.tensor.matmul(tile_cols(root_ps[q], c), feat_t[0:rows, q, c * P:c * P + P],
                                                w[:, :], start=True, stop=True)
                    last.then_inc(root_done[k], 1)

            def node_phase(k):
                if k > 0:
                    pe.wait_ge(fix_ready, k)
                if k == 1:
                    pe.wait_ge(s_noderow, 1)
                skewed_loop(pe, NITERS, NRING, lambda i, q, first: transpose_batch(k, i, q, first),
                            lambda i, q, first: product_batch(k, i, q, first))

            def edge_phase(k):
                if k != 2:
                    pe.wait_ge(store_ready[k], NBATCHES)
                pe.wait_ge(root_kept[k], NBATCHES)
                if k == 0:
                    nc.tensor.matmul(count_ps[0:HI, 0:P], zeros_b[:, 0:HI], zeros_b[:, :], start=True, stop=False)

                def layer01(i, first):
                    w = (wt["w1_edge"], wt["w2_edge"])[k]
                    for r in range(RING):
                        pe.wait_ge(attr_loaded[k][r], (i + 1) * 16)
                        if not first:
                            pe.wait_ge(combined[k], (i - 1) * RING + r + 1)
                        for c in range(SB):
                            last = nc.tensor.matmul(term[r][:, c * D:c * D + D],
                                                    attr_ring[0:DE0, r, c * P:c * P + P], w[:, :],
                                                    start=True, stop=True)
                        last.then_inc(term_ready[k], 1)
                        if k == 0:
                            pe.wait_ge(s_hot, i * RING + r + 1)
                            for c in range(SB):
                                last = nc.tensor.matmul(count_ps[0:HI, 0:P], hi_hot[:, r, c, :],
                                                        lo_hot[:, r, c, :], start=False, stop=False)
                            last.then_inc(s_hist, 1)

                def hidden(i, r, first):
                    pe.wait_ge(attr_loaded[k][r], (i + 1) * 16)
                    if not (first and r == 0):
                        pe.wait_ge(hid_ready, i * RING + r)
                    nc.tensor.matmul(hid_ps[0][0:D, :], wt["w3_h"][:, :], attr_ring[0:DE1P, r, 0:HALF * P],
                                     start=True, stop=True)
                    nc.tensor.matmul(hid_ps[1][0:D, 0:(SB - HALF) * P], wt["w3_h"][:, :],
                                     attr_ring[0:DE1P, r, HALF * P:SB * P],
                                     start=True, stop=True).then_inc(hid_mm, 1)

                def edge_weights(i, r, first):
                    pe.wait_ge(hid_ready, i * RING + r + 1)
                    if not first:
                        pe.wait_ge(combined[k], (i - 1) * RING + r + 1)
                    for c in range(SB):
                        last = nc.tensor.matmul(term[r][:, c * D:c * D + D],
                                                hid_ring[:, r, c * P:c * P + P], wt["w3_e"][:, :],
                                                start=True, stop=True)
                    last.then_inc(term_ready[k], 1)

                if k == 2:
                    skewed_loop(pe, ITERS, RING, hidden, edge_weights)
                else:
                    edge_loop(pe, layer01)

            def stitch(k):
                if k == 0:
                    nc.tensor.matmul(count_ps[0:HI, 0:P], zeros_b[:, 0:HI], zeros_b[:, :], start=False, stop=True
                                     ).then_inc(s_hist_end, 1)
                    pe.wait_ge(s_whole_bc, 1)
                    nc.tensor.matmul(whole_ps[0:D, 0:P], whole_b[:, :], ident[:, :], start=True, stop=True
                                     ).then_inc(s_whole_t, 1)
                pe.wait_ge(scanned[k], BATCHES)
                nc.tensor.transpose(tail_ps[0:D, 0:P], state_ring[:, RING - 1, SB - 1, :], ident[:, :]
                                    ).then_inc(tail_t, 1)
                pe.wait_ge(ends_ready, k + 1)
                nc.tensor.transpose(shift_ps[:, 0:D], ends[:, 0:P], ident[0:D, 0:D]).then_inc(ends_back, 1)
                if k == 0:
                    pe.wait_ge(s_total, 1)
                    nc.tensor.matmul(before_ps[0:HI, 0:1], upper[0:HI, 0:HI], total[:, :], start=True, stop=True
                                     ).then_inc(s_before, 1)

            node_phase(0)
            for k in LAYERS:
                edge_phase(k)
                stitch(k)
                node_phase(k + 1)

        @block.scalar
        def _(act):
            for name, source, _ in weight_srcs:
                act.dma_start(wt[name][:, :], source).then_inc(s_weights, 16)
            act.dma_start(b3_sb[:, :], b3_h).then_inc(s_weights, 16)

            def keep_resid(k, i, q):
                if k == 0:
                    act.wait_ge(agg_loaded[0][q], (i + 1) * 16)
                else:
                    act.wait_ge(node_act[2], i * NRING + q + 1)
                source = agg if k == 0 else act_t
                nc.scalar.copy(resid[:, node_cols(i, q)], flat(source[:, q])).then_inc(resid_kept[k], 1)

            def node_phase(k):
                def relu_rows(i, q, first):
                    b = i * NRING + q
                    keep_resid(k, i, q)
                    act.wait_ge(var_ready[k], b + 1)
                    nc.scalar.activation(std[:, :], mean_var[:, :, 1], ACT.Sqrt, bias=eps[:, 0:1]
                                         ).then_inc(std_ready[k], 1)
                    act.wait_ge(normed[k], b + 1)
                    if not first:
                        act.wait_ge(transposed[k], b - NRING + 1)
                        if k == 2:
                            act.wait_ge(stored[2][q], i * 16)
                    source = act_t if k == 0 else store
                    nc.scalar.activation(flat(feat[:, q]), flat(source[:, q]), ACT.Relu
                                         ).then_inc(feat_ready[k], 1)

                def keep_root(b, q):
                    act.wait_ge(root_done[k], b + 1)
                    if k > 0:
                        act.wait_ge(node_sum[k], b + 1)
                    nc.scalar.copy(root[:, bass.ds(b * (NB * D), HALF * D)], root_ps[q][0][:, 0:HALF * D])
                    nc.scalar.copy(root[:, bass.ds(b * (NB * D) + HALF * D, (NB - HALF) * D)],
                                   root_ps[q][1][:, 0:(NB - HALF) * D]).then_inc(root_kept[k], 1)

                def copies(i, q, first):
                    b = i * NRING + q
                    act.wait_ge(transposed[k], b + 1)
                    if not first:
                        act.wait_ge((msg_done if k == 3 else root_done)[k], b - NRING + 1)
                    nc.scalar.copy(feat_t[0:D, q, 0:HALF * P], tr_ps[0][0:D, :])
                    nc.scalar.copy(feat_t[0:D, q, HALF * P:NB * P], tr_ps[1][0:D, 0:(NB - HALF) * P]
                                   ).then_inc(feat_t_ready[k], 1)
                    if k != 3 and not (first and q == 0):
                        keep_root(b - 1, (q - 1) % NRING)

                skewed_loop(act, NITERS, NRING, relu_rows if k in (0, 2) else lambda i, q, first: None, copies)
                if k != 3:
                    keep_root(NBATCHES - 1, NRING - 1)

            def edge_phase(k):
                def body(i, first):
                    for r in range(RING):
                        b = i * RING + r
                        if not first:
                            act.wait_ge(scanned[k], b - RING + 1)
                        source = keep_mul[:, bass.ds(b * SB, SB)]
                        if k == 2:
                            copy = nc.scalar.copy(keep_ring[:, r, :], source)
                        else:
                            copy = nc.scalar.activation(keep_ring[:, r, :], source, ACT.Identity,
                                                        bias=far_below[:, 0:1], scale=FLT_MAX)
                        if k == 0:
                            copy = nc.scalar.copy(digit_ring[:, r, :, :], digits[:, :, bass.ds(b * SB, SB)])
                        copy.then_inc(keep_copied[k], 1)
                        if k == 2:
                            act.wait_ge(hid_mm, b + 1)
                            if not first:
                                act.wait_ge(term_ready[2], b - RING + 1)
                            nc.scalar.activation(hid_ring[0:D, r, 0:HALF * P], hid_ps[0][0:D, :], ACT.Relu,
                                                 bias=b3_sb[:, 0:1])
                            nc.scalar.activation(hid_ring[0:D, r, HALF * P:SB * P],
                                                 hid_ps[1][0:D, 0:(SB - HALF) * P], ACT.Relu,
                                                 bias=b3_sb[:, 0:1]).then_inc(hid_ready, 1)

                edge_loop(act, body)

            act.wait_ge(s_weights, 16 * NW)
            act.wait_ge(s_zero, 4)
            node_phase(0)
            act.wait_ge(s_setup, 1)
            for k in LAYERS:
                edge_phase(k)
                node_phase(k + 1)

        @block.vector
        def _(dve):
            steps = [0]

            def step(ins):
                steps[0] += 1
                ins.then_inc(s_masks, 1)
                dve.wait_ge(s_masks, steps[0])

            v = nc.vector
            v.memset(zeros[:, :], 0.0).then_inc(s_zero, 1)
            v.memset(ident[:, :], 0.0).then_inc(s_zero, 1)
            v.memset(upper[:, :], 1.0).then_inc(s_zero, 1)
            v.memset(eps[:, :], EPS)
            v.memset(far_below[:, :], -FLT_MAX)
            v.memset(zeros_b[:, :], 0.0)
            v.memset(ends[:, 0:1], 0.0)
            v.memset(hid_ring[D:D + 1, :, :], 1.0)
            v.memset(feat_t[D:D + 2, :, :], 1.0).then_inc(s_zero, 1)

            def setup():
                dve.wait_ge(s_consts, 3)
                dve.wait_ge(s_dst, 16)
                v.tensor_copy(iota_b[:, :], iota_i[:, :])
                step(v.tensor_tensor(keep_mul[:, :], dst_sb[:, 1:T + 1], dst_sb[:, 0:T], ALU.is_equal))
                step(v.tensor_copy(cont_mul[:, :], keep_mul[:, 0:1]))
                v.memset(keep_mul[:, 0:1], 0.0)
                v.tensor_scalar(cont_add[:, :], cont_mul[:, :], 1.0, FLT_MAX, ALU.subtract, ALU.mult)
                step(v.scalar_tensor_tensor(out=work[:, 1:T], in0=keep_mul[:, 1:T], scalar=FAR,
                                            in1=slot_i[:, 1:T], op0=ALU.mult, op1=ALU.add))
                step(v.tensor_reduce(fix[:, :], work[:, 1:T], AX.X, ALU.min))
                step(v.tensor_scalar(whole[:, :], fix[:, :], FAR, None, ALU.is_ge))
                step(v.tensor_tensor(whole[:, :], whole[:, :], cont_mul[:, :], ALU.mult))
                v.tensor_scalar(whole_b[:, :], zeros[:, 0:D], whole[:, 0:1], None, ALU.add
                                ).then_inc(s_whole_bc, 1)
                step(v.tensor_scalar(fix[:, :], fix[:, :], float(T), 1.0, ALU.min, ALU.subtract))
                step(v.tensor_tensor(fix_row[:, :], fix[:, :], first_i[:, :], ALU.add))
                step(v.tensor_scalar(digits[:, 0, :], dst_sb[:, 1:T + 1], LO_MASK, None, ALU.bitwise_and))
                v.tensor_scalar(digits[:, 1, :], dst_sb[:, 1:T + 1], HI_SHIFT, None, ALU.logical_shift_right
                                ).then_inc(s_setup, 1)

            def layernorm(k, i, q, first, source, dest):
                b = i * NRING + q
                if not (first and q == 0):
                    dve.wait_ge(normed[k], b)
                for c in range(NB):
                    last = v.bn_stats(stats[:, c, :], source[:, q, c, :])
                last.then_inc(stat_step[k], 1)
                dve.wait_ge(stat_step[k], 2 * b + 1)
                dve.sem_inc(aggr_turn, 1)
                for c in range(NB):
                    last = v.bn_aggr(mean_var[:, c, :], stats[:, c, :])
                last.then_inc(var_ready[k], 1)
                dve.wait_ge(std_ready[k], b + 1)
                v.reciprocal(rstd[:, :], std[:, :]).then_inc(stat_step[k], 1)
                dve.wait_ge(stat_step[k], 2 * b + 2)
                if not first:
                    dve.wait_ge(feat_ready[k], b - NRING + 1)
                for c in range(NB):
                    last = v.tensor_scalar(dest[:, q, c, :], source[:, q, c, :], mean_var[:, c, 0:1],
                                           rstd[:, c:c + 1], ALU.subtract, ALU.mult)
                last.then_inc(normed[k], 1)

            def node_phase(k):
                def norm_x(i, q, first):
                    dve.wait_ge(agg_loaded[0][q], (i + 1) * 16)
                    layernorm(0, i, q, first, agg, act_t)

                def convolved(i, q, first):
                    b = i * NRING + q
                    dve.wait_ge(agg_loaded[k][q], (i + 1) * 16 * NB)
                    if k == 2 and not first:
                        dve.wait_ge(resid_kept[2], b - NRING + 1)
                        dve.wait_ge(normed[2], b - NRING + 1)
                    v.tensor_tensor(flat(act_t[:, q]), flat(agg[:, q]), root[:, node_cols(i, q)],
                                    ALU.add).then_inc(node_sum[k], 1)
                    dve.wait_ge(node_sum[k], b + 1)
                    if not first:
                        dve.wait_ge(transposed[1] if k == 1 else feat_ready[2], b - NRING + 1)
                    dest = feat if k == 1 else store
                    v.scalar_tensor_tensor(out=flat(dest[:, q]), in0=flat(act_t[:, q]), scalar=SLOPE,
                                           in1=flat(act_t[:, q]), op0=ALU.mult, op1=ALU.max
                                           ).then_inc(feat_ready[1] if k == 1 else conv_act, 1)

                def stage_rows(i, q, first):
                    dve.wait_ge(msg_done[k], i * NRING + q + 1)
                    if not first:
                        dve.wait_ge(stored[k][q], i * 16)
                    v.tensor_copy(flat(store[:, q, 0:HALF, :]), msg_ps[0][:, 0:HALF * D])
                    v.tensor_copy(flat(store[:, q, HALF:NB, :]), msg_ps[1][:, 0:(NB - HALF) * D]
                                  ).then_inc(store_ready[k], 1)

                def second_layer(i, first):
                    for q in range(NRING):
                        convolved(i, q, first)
                        b = i * NRING + q
                        dve.wait_ge(conv_act, b + 1)
                        v.tensor_tensor(flat(act_t[:, q]), flat(store[:, q]), resid[:, node_cols(i, q)],
                                        ALU.add).then_inc(node_act[2], 1)
                        dve.wait_ge(node_act[2], b + 1)
                        layernorm(2, i, q, first, act_t, store)

                def output(i, first):
                    for q in range(NRING):
                        b = i * NRING + q
                        dve.wait_ge(msg_done[3], b + 1)
                        cols = b * (NB * D)
                        v.tensor_tensor(flat(act_t[:, q, 0:HALF, :]), msg_ps[0][:, 0:HALF * D],
                                        root[:, bass.ds(cols, HALF * D)], ALU.add)
                        v.tensor_tensor(flat(act_t[:, q, HALF:NB, :]), msg_ps[1][:, 0:(NB - HALF) * D],
                                        root[:, bass.ds(cols + HALF * D, (NB - HALF) * D)], ALU.add
                                        ).then_inc(node_sum[3], 1)
                        dve.wait_ge(node_sum[3], b + 1)
                        if not first:
                            dve.wait_ge(stored[3][q], i * 16)
                        v.scalar_tensor_tensor(out=flat(store[:, q]), in0=flat(act_t[:, q]), scalar=0.0,
                                               in1=resid[:, node_cols(i, q)], op0=ALU.max, op1=ALU.add
                                               ).then_inc(store_ready[3], 1)

                if k < 2:
                    skewed_loop(dve, NITERS, NRING, (norm_x, convolved)[k], stage_rows)
                else:
                    node_loop(dve, (second_layer, output)[k - 2])

            def edge_phase(k):
                join, op0, op1 = (ALU.mult, ALU.mult, ALU.add) if k == 2 else (ALU.add, ALU.add, ALU.max)
                v.memset(state_ring[:, RING - 1, SB - 1, :], 0.0).then_inc(state_init[k], 1)
                dve.wait_ge(state_init[k], 1)

                def body(i, first):
                    for r in range(RING):
                        b = i * RING + r
                        dve.wait_ge(keep_copied[k], b + 1)
                        if k == 0:
                            if not first:
                                dve.wait_ge(s_hist, b - RING + 1)
                            v.tensor_tensor(lo_hot[:, r], digit_ring[:, r, 0, :, None].to_broadcast([P, SB, P]),
                                            iota_b[:, None, :].to_broadcast([P, SB, P]), ALU.is_equal)
                            v.tensor_tensor(hi_hot[:, r], digit_ring[:, r, 1, :, None].to_broadcast([P, SB, HI]),
                                            iota_b[:, None, 0:HI].to_broadcast([P, SB, HI]), ALU.is_equal
                                            ).then_inc(s_hot, 1)
                        dve.wait_ge(term_ready[k], b + 1)
                        dve.wait_ge(gathered[k][r], (i + 1) * 16 * SB)
                        v.tensor_tensor(flat(rows_ring[:, r]), term[r][:, 0:BD], flat(rows_ring[:, r]), join
                                        ).then_inc(combined[k], 1)
                        dve.wait_ge(combined[k], b + 1)
                        if not first:
                            dve.wait_ge(dumped[k][r], i * 16)
                        for c in range(SB):
                            if c:
                                before_this = state_ring[:, r, c - 1, :]
                                dve.wait_ge(state_step[k], b * (SB - 1) + c)
                            else:
                                before_this = state_ring[:, (r - 1) % RING, SB - 1, :]
                                if not (first and r == 0):
                                    dve.wait_ge(scanned[k], b)
                            v.scalar_tensor_tensor(out=state_ring[:, r, c, :], in0=before_this,
                                                   scalar=keep_ring[:, r, c:c + 1], in1=rows_ring[:, r, c, :],
                                                   op0=op0, op1=op1
                                                   ).then_inc(state_step[k] if c < SB - 1 else scanned[k], 1)

                edge_loop(dve, body)

            def stitch(k):
                op0, op1 = (ALU.mult, ALU.add) if k == 2 else (ALU.add, ALU.max)
                whole_row = whole_mul if k == 2 else whole_add
                if k == 0:
                    dve.wait_ge(s_whole_t, 1)
                    v.tensor_copy(whole_mul[:, :], whole_ps[0:D, 0:P])
                    v.tensor_scalar(whole_add[:, :], whole_ps[0:D, 0:P], 1.0, FLT_MAX, ALU.subtract, ALU.mult
                                    ).then_inc(s_whole_m, 1)
                    dve.wait_ge(s_whole_m, 1)
                dve.wait_ge(tail_t, k + 1)
                v.tensor_tensor_scan(ends[:, 1:P + 1], whole_row[:, :], tail_ps[0:D, 0:P], 0.0, op0, op1
                                     ).then_inc(ends_ready, 1)
                dve.wait_ge(ends_back, k + 1)
                dve.wait_ge(fix_loaded, 16 * (k + 1))
                cont = cont_mul if k == 2 else cont_add
                v.scalar_tensor_tensor(out=fix_vals[:, :], in0=shift_ps[:, 0:D], scalar=cont[:, 0:1],
                                       in1=fix_vals[:, :], op0=op0, op1=op1).then_inc(fix_ready, 1)

            def node_rows():
                seen = [0]

                def step(ins):
                    seen[0] += 1
                    ins.then_inc(s_pref, 1)
                    dve.wait_ge(s_pref, seen[0])

                dve.wait_ge(s_hist_end, 1)
                step(v.tensor_copy(count[:, :], count_ps[0:HI, 0:P]))
                v.tensor_reduce(total[:, :], count[:, :], AX.X, ALU.add).then_inc(s_total, 1)
                v.tensor_tensor_scan(prefix[:, :], count[:, :], zeros[0:HI, :], 0.0, ALU.add, ALU.add)
                v.tensor_scalar(empty[:, :], count[:, :], 0.0, None, ALU.is_equal)
                dve.wait_ge(s_before, 1)
                step(v.tensor_copy(before[:, :], before_ps[0:HI, 0:1]))
                step(v.tensor_scalar(prefix[:, :], prefix[:, :], before[:, 0:1], 1.0, ALU.add, ALU.subtract))
                step(v.tensor_scalar(node_row_f[:, :], prefix[:, :], -1.0, float(ZERO_ROW), ALU.mult, ALU.add))
                step(v.tensor_tensor(node_row_f[:, :], node_row_f[:, :], empty[:, :], ALU.mult))
                v.tensor_tensor(node_row_i[:, :], node_row_f[:, :], prefix[:, :], ALU.add
                                ).then_inc(s_noderow, 1)

            node_phase(0)
            setup()
            for k in LAYERS:
                edge_phase(k)
                stitch(k)
                if k == 0:
                    node_rows()
                node_phase(k + 1)


def kernel(**inputs):
    import numpy as _np
    import concourse.bacc as _bacc
    from concourse import mybir as _mybir
    from concourse.bass_utils import run_bass_kernel_spmd as _run

    def get(name):
        return _np.asarray(inputs[name])

    def edge_attr(name, rows):
        a = get(name)
        w = a.shape[1]
        a = _np.pad(a, ((0, P * T - E), (0, rows - w)))
        return a.reshape(P, T, rows).transpose(2, 1, 0).reshape(rows, T * P)

    def rows(*parts):
        return _np.concatenate([_np.atleast_2d(a) for a in parts], axis=0)

    arrays = {
        "x": _np.pad(get("x"), ((0, NPAD - N), (0, 0))).reshape(P, NT * D),
        "src": _np.pad(get("src"), (0, P * T - E)).reshape(P, T),
        "dst": _np.pad(_np.pad(get("dst"), (1, 0), constant_values=-1), (0, P * T - E), constant_values=N),
        "ea32": edge_attr("edge_attr_32", DE0),
        "ea17": edge_attr("edge_attr_17", DE1P),
        "w1_msg": get("L0_gnn_W1_msg"),
        "w1_root": rows(get("L0_gnn_W1_root"), get("L0_gnn_b1")),
        "w1_edge": get("L0_gnn_W1_edge"),
        "w2_msg": get("L0_gnn_W2_msg"),
        "w2_root": rows(get("L0_gnn_W2_root"), get("L0_gnn_b2")),
        "w2_edge": get("L0_gnn_W2_edge"),
        "w3_h": _np.pad(get("L1_gnn_W1").T, ((0, DE1P - DE1), (0, 0))),
        "b3_h": get("L1_gnn_b1").reshape(D, 1),
        "w3_e": rows(get("L1_gnn_W2").T, get("L1_gnn_b2")),
        "w3_self": rows(get("L1_gnn_Ws").T, get("L1_gnn_bs"), get("L1_gnn_bn")),
        "w3_nbr": get("L1_gnn_Wn").T,
    }
    nc = _bacc.Bacc("TRN2", target_bir_lowering=False, num_devices=1)
    in_map, args = {}, []
    for name, a in arrays.items():
        a = _np.ascontiguousarray(a)
        in_map[f"in_{name}"] = a
        args.append(nc.dram_tensor(f"in_{name}", a.shape, _mybir.dt.from_np(a.dtype), kind="ExternalInput").ap())
    out = nc.dram_tensor("out_nodes", (P, NT * D), F32, kind="ExternalOutput").ap()
    gnn_program(nc, *args, out)
    r = _run(nc, [in_map], core_ids=[0])
    return r.results[0]["out_nodes"].reshape(NPAD, D)[:N]
```

```python
from contextlib import ExitStack

import concourse.bass as bass
from concourse import mybir

ALU = mybir.AluOpType
ACT = mybir.ActivationFunctionType
AX = mybir.AxisListType
F32 = mybir.dt.float32
BF16 = mybir.dt.bfloat16
I32 = mybir.dt.int32

P = 128
N, D, E = 12500, 96, 412500
DE0, DE1 = 32, 17
DE1P = 18

SB = 5
RING = 3
T = -(-E // (P * SB * RING)) * SB * RING
ITERS = T // (SB * RING)
BATCHES = ITERS * RING
BD = SB * D
ZERO_ROW = P * T

NT = -(-N // P)
NPAD = NT * P
NB = 7
NRING = 2
NITERS = NT // (NB * NRING)
NBATCHES = NITERS * NRING
HALF = 4

HI = -(-N // P)
HI_SHIFT, LO_MASK = 7, 127

EPS = 1e-5
SLOPE = 0.01
FLT_MAX = 3.4028234663852886e38
FAR = float(1 << 20)

assert NT % (NB * NRING) == 0 and NITERS > 3 and ITERS > 3


def gnn_program(nc, x, src, dst, ea32, ea17, w1_msg, w1_root, w1_edge, w2_msg, w2_root, w2_edge,
                w3_h, b3_h, w3_e, w3_self, w3_nbr, out):
    with ExitStack() as ctx:
        def sb(name, shape, dt=F32):
            return ctx.enter_context(nc.sbuf_tensor(name, shape, dt))

        def sem(name):
            return ctx.enter_context(nc.semaphore(name))

        def dram(name, shape, dt=F32):
            return nc.dram_tensor(name, shape, dt).ap()

        table = [dram(f"table{k}", [NPAD, D]) for k in range(3)]
        running = dram("running", [P * T + 1, D])
        feat_dram = [dram(f"feat_dram{k}", [D, NPAD]) for k in range(3)]
        node_row_dram = dram("node_row_dram", [HI, P], I32)

        running_v = running[0:P * T, :].rearrange("(p t) f -> p (t f)", p=P)
        table_v = [t.rearrange("(p t) f -> p (t f)", p=P) for t in table]
        node_row_v = node_row_dram.rearrange("h l -> (h l)").rearrange("(p t) -> p t", p=P)

        wt = {}
        weight_srcs = [("w1_msg", w1_msg, D), ("w1_root", w1_root, D + 1), ("w1_edge", w1_edge, DE0),
                       ("w2_msg", w2_msg, D), ("w2_root", w2_root, D + 1), ("w2_edge", w2_edge, DE0),
                       ("w3_h", w3_h, DE1P), ("w3_e", w3_e, D + 1), ("w3_self", w3_self, D + 2),
                       ("w3_nbr", w3_nbr, D)]
        for name, _, rows in weight_srcs:
            wt[name] = sb(name + "_sb", [rows, D])
        b3_sb = sb("b3_sb", [D, 1])

        resid = sb("resid", [P, NT * D])
        keep_mul = sb("keep_mul", [P, T])
        digits = sb("digits", [P, 2, T], I32)
        dst_sb = sb("dst_sb", [P, T + 1], I32)
        slot_i = digits[:, 0, :]
        work = digits[:, 1, :].bitcast(F32)

        src_ring = sb("src_ring", [P, RING, SB], I32)
        rows_ring = sb("rows_ring", [P, RING, SB, D])
        state_ring = sb("state_ring", [P, RING, SB, D])
        attr_ring = sb("attr_ring", [DE0, RING, SB * P])
        keep_ring = sb("keep_ring", [P, RING, SB])
        digit_ring = sb("digit_ring", [P, RING, 2, SB], BF16)
        lo_hot = sb("lo_hot", [P, RING, SB, P], BF16)
        hi_hot = sb("hi_hot", [P, RING, SB, HI], BF16)
        hid_ring = sb("hid_ring", [D + 1, RING, SB * P])

        row_ring = sb("row_ring", [P, NRING, NB], I32)
        agg = sb("agg", [P, NRING, NB, D])
        act_t = sb("act_t", [P, NRING, NB, D])
        feat = sb("feat", [P, NRING, NB, D])
        feat_t = sb("feat_t", [D, NRING, NB * P])
        prev_t = sb("prev_t", [D + 2, NRING, NB * P])
        store = sb("store", [P, NRING, NB, D])
        stats = sb("stats", [P, NB, 6])
        mean_var = sb("mean_var", [P, NB, 2])
        std = sb("std", [P, NB])
        rstd = sb("rstd", [P, NB])
        eps = sb("eps", [P, 1])
        far_below = sb("far_below", [P, 1])

        ident = sb("ident", [P, P])
        iota_i = sb("iota_i", [P, P], I32)
        iota_b = sb("iota_b", [P, P], BF16)
        first_i = sb("first_i", [P, 1], I32)
        upper = sb("upper", [P, P])
        cont_mul = sb("cont_mul", [P, 1])
        cont_add = sb("cont_add", [P, 1])
        whole = sb("whole", [P, 1])
        whole_b = sb("whole_b", [P, D])
        whole_mul = sb("whole_mul", [D, P])
        whole_add = sb("whole_add", [D, P])
        fix = sb("fix", [P, 1])
        fix_row = sb("fix_row", [P, 1], I32)
        fix_vals = sb("fix_vals", [P, D])
        ends = sb("ends", [D, P + 1])
        count = sb("count", [HI, P])
        total = sb("total", [HI, 1])
        before = sb("before", [HI, 1])
        prefix = sb("prefix", [HI, P])
        empty = sb("empty", [HI, P])
        node_row_f = sb("node_row_f", [HI, P])
        node_row_i = sb("node_row_i", [HI, P], I32)
        zeros = sb("zeros", [P, P])
        zeros_b = sb("zeros_b", [P, P], BF16)

        bank = [ctx.enter_context(nc.psum_tensor(f"bank{k}", [P, 512], F32)) for k in range(8)]
        term = bank[0:RING]
        hid_ps = bank[3:5]
        count_ps = bank[7]
        tail_ps, shift_ps, whole_ps, before_ps = bank[3], bank[4], bank[5], bank[6]
        tr_ps = bank[0:2]
        msg_ps = bank[2:4]
        root_ps = [bank[4:6], bank[6:8]]

        block = ctx.enter_context(nc.Block())

        s_w1_msg = sem("first_table_weights_loaded")
        s_weights = sem("other_weights_loaded")
        s_x_first = sem("first_rows_of_x_loaded")
        s_x_rest = sem("other_rows_of_x_loaded")
        s_dst = sem("dst_loaded")
        s_consts = sem("pool_consts_ready")
        s_zero = sem("vector_consts_ready")
        s_ident = sem("identity_ready")
        s_keep = sem("keep_step")
        s_ones = sem("ones_row_ready")
        s_masks = sem("masks_step")
        s_setup = sem("segment_layout_ready")
        s_whole_bc = sem("whole_broadcast_ready")
        s_whole_t = sem("whole_transposed")
        s_table = sem("function_table_loaded")
        s_zrow = sem("zero_row_written")
        s_hot = sem("one_hots_ready")
        s_hist = sem("one_hots_counted")
        s_hist_end = sem("histogram_complete")
        s_pref = sem("prefix_step")
        s_total = sem("totals_ready")
        s_before = sem("counts_before_ready")
        s_noderow = sem("node_rows_ready")
        s_noderow_w = sem("node_rows_written")

        LAYERS = range(3)
        src_loaded = [[sem(f"src_loaded_{k}_{r}") for r in range(RING)] for k in LAYERS]
        attr_loaded = [[sem(f"attr_loaded_{k}_{r}") for r in range(RING)] for k in LAYERS]
        gathered = [[sem(f"gathered_{k}_{r}") for r in range(RING)] for k in LAYERS]
        dumped = [[sem(f"dumped_{k}_{r}") for r in range(RING)] for k in LAYERS]
        gather_turn = sem("gather_turn")
        keep_copied = [sem(f"keep_copied_{k}") for k in LAYERS]
        term_ready = [sem(f"term_ready_{k}") for k in LAYERS]
        combined = [sem(f"messages_ready_{k}") for k in LAYERS]
        state_step = [sem(f"state_step_{k}") for k in LAYERS]
        scanned = [sem(f"batch_scanned_{k}") for k in LAYERS]
        state_init = [sem(f"state_init_{k}") for k in LAYERS]
        hid_mm = sem("hidden_product_ready")
        hid_ready = sem("hidden_ready")
        tail_t = sem("tails_transposed")
        ends_ready = sem("ends_scanned")
        ends_back = sem("ends_transposed_back")
        fix_loaded = sem("fix_rows_loaded")
        fix_ready = sem("fix_rows_ready")
        fix_stored = sem("fix_rows_stored")
        PHASES = range(4)
        rowidx_loaded = [[sem(f"node_rows_loaded_{k}_{q}") for q in range(NRING)] if k else None for k in PHASES]
        agg_loaded = [[sem(f"aggregates_loaded_{k}_{q}") for q in range(NRING)] if k else None for k in PHASES]
        agg_turn = sem("aggregate_turn")
        node_sum = {k: sem(f"node_sum_{k}") for k in (1, 2)}
        node_act = {k: sem(f"node_activated_{k}") for k in (2,)}
        out_sum = sem("output_sum")
        conv_act = sem("second_convolution_activated")
        stat_step = {k: sem(f"layernorm_step_{k}") for k in (0, 2)}
        aggr_turn = sem("layernorm_turn")
        var_ready = {k: sem(f"variance_ready_{k}") for k in (0, 2)}
        std_ready = {k: sem(f"deviation_ready_{k}") for k in (0, 2)}
        normed = {k: sem(f"normalised_{k}") for k in (0, 2)}
        feat_ready = {k: sem(f"features_ready_{k}") for k in (0, 1, 2)}
        resid_kept = {2: sem("residual_kept_2")}
        transposed = [sem(f"features_transposed_{k}") for k in PHASES]
        feat_t_ready = [sem(f"transposed_features_ready_{k}") for k in PHASES]
        msg_done = {k: sem(f"message_products_ready_{k}") for k in (0, 1, 3)}
        root_done = {k: sem(f"root_products_ready_{k}") for k in (1, 2, 3)}
        root_kept = sem("root_terms_kept")
        feat_stored = {k: [sem(f"features_stored_{k}_{q}") for q in range(NRING)] for k in (0, 1, 2)}
        prev_loaded = {k: [sem(f"features_loaded_{k}_{q}") for q in range(NRING)] for k in (1, 2, 3)}
        store_ready = [sem(f"store_rows_ready_{k}") for k in PHASES]
        stored = [[sem(f"rows_stored_{k}_{q}") for q in range(NRING)] for k in PHASES]

        NW = len(weight_srcs)
        MSG_W = [wt["w1_msg"], wt["w2_msg"], None, wt["w3_nbr"]]
        ROOT_W = [None, (wt["w1_root"], D + 1), (wt["w2_root"], D + 1), (wt["w3_self"], D + 2)]

        def flat(ap):
            return ap.rearrange("p n f -> p (n f)")

        def tile_cols(banks, k):
            return banks[k // HALF][:, (k % HALF) * D:(k % HALF) * D + D]

        def edge_loop(eng, body):
            body(0, True)
            with eng.Fori(1, ITERS) as i:
                body(i, False)

        def node_loop(eng, body):
            body(0, True)
            with eng.Fori(1, NITERS) as i:
                body(i, False)

        def skewed_loop(eng, iters, ring, lead, follow, ahead=1, start=None):
            peeled = (ring - 1 + ahead) // ring

            def body(i, first, left):
                for r in range(ring):
                    if start:
                        start(i, r, first)
                    on, to = divmod(r + ahead, ring)
                    if on < left:
                        lead(i + on, to, first and on == 0)
                    follow(i, r, first)

            for j in range(ahead):
                lead(j // ring, j % ring, j < ring)
            body(0, True, iters)
            with eng.Fori(1, iters - peeled) as i:
                body(i, False, iters)
            for i in range(iters - peeled, iters):
                body(i, False, iters - i)

        def node_batch_t(i, q):
            return bass.ds((i * NRING + q) * (NB * P), NB * P)

        def node_cols(i, q):
            return bass.ds((i * NRING + q) * (NB * D), NB * D)

        @block.sync
        def _(sp):
            def node_phase(k):
                def loads(i, q, first):
                    if not first:
                        sp.wait_ge(agg_loaded[k][q], i * 16 * NB)
                    sp.dma_start(row_ring[:, q, :], node_row_v[:, bass.ds((i * NRING + q) * NB, NB)]
                                 ).then_inc(rowidx_loaded[k][q], 16)
                    if not first:
                        sp.wait_ge(root_done[k], (i - 1) * NRING + q + 1)
                    sp.dma_start(prev_t[0:D, q, :], feat_dram[k - 1][:, node_batch_t(i, q)]
                                 ).then_inc(prev_loaded[k][q], 16)

                def stores(i, q, first):
                    if first and q == 0 and k < 3:
                        first_loads(k)
                    if k < 3:
                        sp.wait_ge(feat_t_ready[k], i * NRING + q + 1)
                        sp.dma_start(feat_dram[k][:, node_batch_t(i, q)], feat_t[:, q, :]
                                     ).then_inc(feat_stored[k][q], 16)
                    sp.wait_ge(feat_ready[2] if k == 2 else store_ready[k], i * NRING + q + 1)
                    dest = out[:, node_cols(i, q)] if k == 3 else table_v[k][:, node_cols(i, q)]
                    source = feat if k == 2 else store
                    sp.dma_start(dest, flat(source[:, q])).then_inc(stored[k][q], 16)

                if k == 0:
                    cut = NRING * NB * D
                    sp.dma_start(resid[:, 0:cut], x[:, 0:cut]).then_inc(s_x_first, 16)
                    sp.dma_start(resid[:, cut:NT * D], x[:, cut:NT * D]).then_inc(s_x_rest, 16)
                    sp.dma_start(dst_sb[:, :], bass.AP(tensor=dst.tensor, offset=0, ap=[[T, P], [1, T + 1]])
                                 ).then_inc(s_dst, 16)
                    for name, source, _ in weight_srcs[1:]:
                        sp.dma_start(wt[name][:, :], source).then_inc(s_weights, 16)
                    sp.dma_start(b3_sb[:, :], b3_h).then_inc(s_weights, 16)
                    sp.wait_ge(s_zero, 3)
                    sp.dma_start(running[P * T:P * T + 1, :], zeros[0:1, 0:D]).then_inc(s_zrow, 16)
                    node_loop(sp, lambda i, first: [stores(i, q, first) for q in range(NRING)])
                    return
                if k == 1:
                    sp.wait_ge(s_noderow, 1)
                    sp.dma_start(node_row_dram[:, :], node_row_i[:, :]).then_inc(s_noderow_w, 16)
                    sp.wait_ge(s_noderow_w, 16)
                for q in range(NRING):
                    sp.wait_ge(feat_stored[k - 1][q], 16 * NITERS)
                if k > 1:
                    sp.wait_ge(root_done[k - 1], NBATCHES)
                skewed_loop(sp, NITERS, NRING, loads, stores, ahead=NRING + 1)

            def load_src(k, b, r):
                sp.dma_start(src_ring[:, r, :], src[:, bass.ds(b * SB, SB)]).then_inc(src_loaded[k][r], 16)

            def load_attr(k, b, r):
                attr, width = (ea17, DE1P) if k == 2 else (ea32, DE0)
                sp.dma_start(attr_ring[0:width, r, :], attr[:, bass.ds(b * (SB * P), SB * P)]
                             ).then_inc(attr_loaded[k][r], 16)

            def first_loads(k):
                if k > 0:
                    sp.wait_ge(term_ready[k - 1], BATCHES)
                for r in range(RING):
                    if k > 0:
                        sp.wait_ge(gathered[k - 1][r], 16 * SB * ITERS)
                    load_src(k, r, r)
                    load_attr(k, r, r)

            def edge_phase(k):
                def body(i, more):
                    for r in range(RING):
                        if more:
                            sp.wait_ge(gathered[k][r], (i + 1) * 16 * SB)
                            load_src(k, (i + 1) * RING + r, r)
                            sp.wait_ge(hid_mm if k == 2 else term_ready[k], i * RING + r + 1)
                            load_attr(k, (i + 1) * RING + r, r)
                        sp.wait_ge(scanned[k], i * RING + r + 1)
                        sp.dma_start(running_v[:, bass.ds((i * RING + r) * BD, BD)], flat(state_ring[:, r])
                                     ).then_inc(dumped[k][r], 16)

                with sp.Fori(0, ITERS - 1) as i:
                    body(i, True)
                body(ITERS - 1, False)

            node_phase(0)
            for k in LAYERS:
                edge_phase(k)
                node_phase(k + 1)
            for q in range(NRING):
                sp.wait_ge(stored[3][q], 16 * NITERS)

        @block.gpsimd
        def _(pool):
            pool.iota(iota_i[:, :], [[1, P]], base=0, channel_multiplier=0).then_inc(s_consts, 1)
            pool.iota(first_i[:, :], [[0, 1]], base=0, channel_multiplier=T).then_inc(s_consts, 1)
            pool.iota(slot_i, [[1, T]], base=0, channel_multiplier=0).then_inc(s_consts, 1)
            pool.wait_ge(s_zero, 4)
            pool.affine_select(out=ident[:, :], in_=ident[:, :], compare_op=ALU.not_equal, fill=1.0,
                               base=0, pattern=[[-1, P]], channel_multiplier=1).then_inc(s_ident, 1)
            pool.affine_select(out=upper[:, :], in_=upper[:, :], compare_op=ALU.is_gt, fill=0.0,
                               base=0, pattern=[[1, P]], channel_multiplier=-1).then_inc(s_ident, 1)
            pool.wait_ge(s_dst, 16)
            nc.gpsimd.tensor_tensor(digits[:, 1, :], dst_sb[:, 1:T + 1], dst_sb[:, 0:T], ALU.subtract
                                    ).then_inc(s_keep, 1)
            pool.wait_ge(s_keep, 1)
            nc.gpsimd.tensor_scalar(keep_mul[:, :], digits[:, 1, :], 0.0, None, ALU.is_equal).then_inc(s_keep, 1)
            pool.wait_ge(s_keep, 2)
            nc.gpsimd.tensor_copy(cont_mul[:, :], keep_mul[:, 0:1]).then_inc(s_keep, 1)
            pool.wait_ge(s_keep, 3)
            nc.gpsimd.memset(keep_mul[:, 0:1], 0.0).then_inc(s_keep, 1)
            pool.wait_ge(s_keep, 4)
            nc.gpsimd.memset(hid_ring[D:D + 1, :, :], 1.0).then_inc(s_ones, 1)

            def edge_phase(k):
                for q in range(NRING):
                    pool.wait_ge(stored[k][q], 16 * NITERS)

                def body(i, first):
                    for r in range(RING):
                        pool.wait_ge(src_loaded[k][r], (i + 1) * 16)
                        if not first:
                            pool.wait_ge(scanned[k], (i - 1) * RING + r + 1)
                        pool.sem_inc(gather_turn, 1)
                        for c in range(SB):
                            pool.indirect_dma_start(
                                rows_ring[:, r, c, :], None, table[k][:, :],
                                bass.IndirectOffsetOnAxis(ap=src_ring[:, r, c:c + 1], axis=0),
                            ).then_inc(gathered[k][r], 16)

                edge_loop(pool, body)

            def stitch(k):
                for r in range(RING):
                    pool.wait_ge(dumped[k][r], 16 * ITERS)
                if k == 0:
                    pool.wait_ge(s_setup, 1)
                pool.indirect_dma_start(fix_vals[:, :], None, running[:, :],
                                        bass.IndirectOffsetOnAxis(ap=fix_row[:, 0:1], axis=0)
                                        ).then_inc(fix_loaded, 16)
                pool.wait_ge(fix_ready, k + 1)
                pool.indirect_dma_start(running[:, :], bass.IndirectOffsetOnAxis(ap=fix_row[:, 0:1], axis=0),
                                        fix_vals[:, :], None).then_inc(fix_stored, 16)
                pool.wait_ge(fix_stored, 16 * (k + 1))
                if k == 0:
                    pool.wait_ge(s_zrow, 16)

            def node_phase(k):
                def body(i, first):
                    for q in range(NRING):
                        pool.wait_ge(rowidx_loaded[k][q], (i + 1) * 16)
                        if not first:
                            free = transposed[3] if k == 3 else node_sum[k]
                            pool.wait_ge(free, (i - 1) * NRING + q + 1)
                        pool.sem_inc(agg_turn, 1)
                        for c in range(NB):
                            pool.indirect_dma_start(
                                agg[:, q, c, :], None, running[:, :],
                                bass.IndirectOffsetOnAxis(ap=row_ring[:, q, c:c + 1], axis=0),
                            ).then_inc(agg_loaded[k][q], 16)

                node_loop(pool, body)

            for k in LAYERS:
                edge_phase(k)
                stitch(k)
                node_phase(k + 1)

        @block.tensor
        def _(pe):
            pe.wait_ge(s_w1_msg, 16)
            pe.wait_ge(s_ident, 1)

            def transpose_batch(k, i, q, first):
                source = agg if k == 3 else feat
                if k == 3:
                    pe.wait_ge(agg_loaded[3][q], (i + 1) * 16 * NB)
                else:
                    pe.wait_ge(feat_ready[k], i * NRING + q + 1)
                if not (first and q == 0):
                    pe.wait_ge(feat_t_ready[k], i * NRING + q)
                for c in range(NB):
                    last = nc.tensor.transpose(tr_ps[c // HALF][0:D, (c % HALF) * P:(c % HALF) * P + P],
                                               source[:, q, c, :], ident[:, :])
                last.then_inc(transposed[k], 1)

            def root_batch(k, i, q, first):
                w, rows = ROOT_W[k]
                pe.wait_ge(prev_loaded[k][q], (i + 1) * 16)
                if not first:
                    pe.wait_ge(node_sum[k] if k < 3 else root_kept, (i - 1) * NRING + q + 1)
                for c in range(NB):
                    last = nc.tensor.matmul(tile_cols(root_ps[q], c), prev_t[0:rows, q, c * P:c * P + P],
                                            w[:, :], start=True, stop=True)
                last.then_inc(root_done[k], 1)

            def message_batch(k, i, q, first):
                pe.wait_ge(feat_t_ready[k], i * NRING + q + 1)
                if not (first and q == 0):
                    pe.wait_ge(store_ready[k], i * NRING + q)
                for c in range(NB):
                    last = nc.tensor.matmul(tile_cols(msg_ps, c), feat_t[:, q, c * P:c * P + P], MSG_W[k][:, :],
                                            start=True, stop=True)
                last.then_inc(msg_done[k], 1)

            def node_phase(k):
                if k > 0:
                    pe.wait_ge(fix_ready, k)
                if k == 1:
                    pe.wait_ge(s_noderow, 1)

                def transposes(i, q, first):
                    transpose_batch(k, i, q, first)

                def roots(i, q, first):
                    root_batch(k, i, q, first)

                def messages(i, q, first):
                    message_batch(k, i, q, first)

                if k == 0:
                    skewed_loop(pe, NITERS, NRING, transposes, messages)
                elif k == 2:
                    skewed_loop(pe, NITERS, NRING, roots, transposes)
                else:
                    skewed_loop(pe, NITERS, NRING, roots, messages, start=transposes)

            def edge_phase(k):
                if k == 0:
                    pe.wait_ge(s_weights, 16 * NW)
                    pe.wait_ge(s_ident, 2)
                pe.wait_ge(feat_t_ready[k], NBATCHES)
                if k in msg_done:
                    pe.wait_ge(store_ready[k], NBATCHES)
                if k in root_done:
                    pe.wait_ge(node_sum[k], NBATCHES)
                if k == 2:
                    pe.wait_ge(s_ones, 1)
                if k == 0:
                    nc.tensor.matmul(count_ps[0:HI, 0:P], zeros_b[:, 0:HI], zeros_b[:, :], start=True, stop=False)

                def layer01(i, first):
                    w = (wt["w1_edge"], wt["w2_edge"])[k]
                    for r in range(RING):
                        pe.wait_ge(attr_loaded[k][r], (i + 1) * 16)
                        if not first:
                            pe.wait_ge(combined[k], (i - 1) * RING + r + 1)
                        for c in range(SB):
                            last = nc.tensor.matmul(term[r][:, c * D:c * D + D],
                                                    attr_ring[0:DE0, r, c * P:c * P + P], w[:, :],
                                                    start=True, stop=True)
                        last.then_inc(term_ready[k], 1)
                        if k == 0:
                            pe.wait_ge(s_hot, i * RING + r + 1)
                            for c in range(SB):
                                last = nc.tensor.matmul(count_ps[0:HI, 0:P], hi_hot[:, r, c, :],
                                                        lo_hot[:, r, c, :], start=False, stop=False)
                            last.then_inc(s_hist, 1)

                def hidden(i, r, first):
                    pe.wait_ge(attr_loaded[k][r], (i + 1) * 16)
                    if not (first and r == 0):
                        pe.wait_ge(hid_ready, i * RING + r)
                    nc.tensor.matmul(hid_ps[0][0:D, :], wt["w3_h"][:, :], attr_ring[0:DE1P, r, 0:HALF * P],
                                     start=True, stop=True)
                    nc.tensor.matmul(hid_ps[1][0:D, 0:(SB - HALF) * P], wt["w3_h"][:, :],
                                     attr_ring[0:DE1P, r, HALF * P:SB * P],
                                     start=True, stop=True).then_inc(hid_mm, 1)

                def edge_weights(i, r, first):
                    pe.wait_ge(hid_ready, i * RING + r + 1)
                    if not first:
                        pe.wait_ge(combined[k], (i - 1) * RING + r + 1)
                    for c in range(SB):
                        last = nc.tensor.matmul(term[r][:, c * D:c * D + D],
                                                hid_ring[:, r, c * P:c * P + P], wt["w3_e"][:, :],
                                                start=True, stop=True)
                    last.then_inc(term_ready[k], 1)

                if k == 2:
                    skewed_loop(pe, ITERS, RING, hidden, edge_weights)
                else:
                    edge_loop(pe, layer01)

            def stitch(k):
                if k == 0:
                    nc.tensor.matmul(count_ps[0:HI, 0:P], zeros_b[:, 0:HI], zeros_b[:, :], start=False, stop=True
                                     ).then_inc(s_hist_end, 1)
                    pe.wait_ge(s_whole_bc, 1)
                    nc.tensor.matmul(whole_ps[0:D, 0:P], whole_b[:, :], ident[:, :], start=True, stop=True
                                     ).then_inc(s_whole_t, 1)
                pe.wait_ge(scanned[k], BATCHES)
                nc.tensor.transpose(tail_ps[0:D, 0:P], state_ring[:, RING - 1, SB - 1, :], ident[:, :]
                                    ).then_inc(tail_t, 1)
                if k == 0:
                    pe.wait_ge(s_total, 1)
                    nc.tensor.matmul(before_ps[0:HI, 0:1], upper[0:HI, 0:HI], total[:, :], start=True, stop=True
                                     ).then_inc(s_before, 1)
                pe.wait_ge(ends_ready, k + 1)
                nc.tensor.transpose(shift_ps[:, 0:D], ends[:, 0:P], ident[0:D, 0:D]).then_inc(ends_back, 1)

            node_phase(0)
            for k in LAYERS:
                edge_phase(k)
                stitch(k)
                node_phase(k + 1)

        @block.scalar
        def _(act):
            act.dma_start(wt["w1_msg"][:, :], w1_msg).then_inc(s_w1_msg, 16)

            def node_phase(k):
                def relu_rows(i, q, first):
                    b = i * NRING + q
                    if k == 2:
                        act.wait_ge(node_act[2], b + 1)
                        nc.scalar.copy(resid[:, node_cols(i, q)], flat(act_t[:, q])).then_inc(resid_kept[2], 1)
                    act.wait_ge(var_ready[k], b + 1)
                    nc.scalar.activation(std[:, :], mean_var[:, :, 1], ACT.Sqrt, bias=eps[:, 0:1]
                                         ).then_inc(std_ready[k], 1)
                    act.wait_ge(normed[k], b + 1)
                    if not first:
                        act.wait_ge(transposed[k], b - NRING + 1)
                        if k == 2:
                            act.wait_ge(stored[2][q], i * 16)
                    source = act_t if k == 0 else store
                    nc.scalar.activation(flat(feat[:, q]), flat(source[:, q]), ACT.Relu
                                         ).then_inc(feat_ready[k], 1)

                def stage_rows(i, q, first):
                    act.wait_ge(msg_done[0], i * NRING + q + 1)
                    if not first:
                        act.wait_ge(stored[0][q], i * 16)
                    nc.scalar.copy(flat(store[:, q, 0:HALF, :]), msg_ps[0][:, 0:HALF * D])
                    nc.scalar.copy(flat(store[:, q, HALF:NB, :]), msg_ps[1][:, 0:(NB - HALF) * D]
                                   ).then_inc(store_ready[0], 1)

                def copies(i, q, first):
                    b = i * NRING + q
                    act.wait_ge(transposed[k], b + 1)
                    if not first:
                        if k in msg_done:
                            act.wait_ge(msg_done[k], b - NRING + 1)
                        if k < 3:
                            act.wait_ge(feat_stored[k][q], i * 16)
                    nc.scalar.copy(feat_t[:, q, 0:HALF * P], tr_ps[0][0:D, :])
                    nc.scalar.copy(feat_t[:, q, HALF * P:NB * P], tr_ps[1][0:D, 0:(NB - HALF) * P]
                                   ).then_inc(feat_t_ready[k], 1)
                    if k == 3:
                        act.wait_ge(root_done[3], b + 1)
                        if not first:
                            act.wait_ge(store_ready[3], b - NRING + 1)
                        nc.scalar.copy(flat(act_t[:, q, 0:HALF, :]), root_ps[q][0][:, 0:HALF * D])
                        nc.scalar.copy(flat(act_t[:, q, HALF:NB, :]), root_ps[q][1][:, 0:(NB - HALF) * D]
                                       ).then_inc(root_kept, 1)
                    if k == 0:
                        if q == 1:
                            stage_rows(i, 0, first)
                        elif not first:
                            stage_rows(i - 1, 1, False)

                def relu_and_copies(i, first):
                    for q in range(NRING):
                        relu_rows(i, q, first)
                        copies(i, q, first)

                if k == 0:
                    skewed_loop(act, NITERS, NRING, relu_rows, copies)
                    stage_rows(NITERS - 1, 1, False)
                elif k == 2:
                    node_loop(act, relu_and_copies)
                else:
                    node_loop(act, lambda i, first: [copies(i, q, first) for q in range(NRING)])

            def edge_phase(k):
                def body(i, first):
                    for r in range(RING):
                        b = i * RING + r
                        if not first:
                            act.wait_ge(scanned[k], b - RING + 1)
                        source = keep_mul[:, bass.ds(b * SB, SB)]
                        if k == 2:
                            copy = nc.scalar.copy(keep_ring[:, r, :], source)
                        else:
                            copy = nc.scalar.activation(keep_ring[:, r, :], source, ACT.Identity,
                                                        bias=far_below[:, 0:1], scale=FLT_MAX)
                        if k == 0:
                            copy = nc.scalar.copy(digit_ring[:, r, :, :], digits[:, :, bass.ds(b * SB, SB)])
                        copy.then_inc(keep_copied[k], 1)
                        if k == 2:
                            act.wait_ge(hid_mm, b + 1)
                            if not first:
                                act.wait_ge(term_ready[2], b - RING + 1)
                            nc.scalar.activation(hid_ring[0:D, r, 0:HALF * P], hid_ps[0][0:D, :], ACT.Relu,
                                                 bias=b3_sb[:, 0:1])
                            nc.scalar.activation(hid_ring[0:D, r, HALF * P:SB * P],
                                                 hid_ps[1][0:D, 0:(SB - HALF) * P], ACT.Relu,
                                                 bias=b3_sb[:, 0:1]).then_inc(hid_ready, 1)

                edge_loop(act, body)

            act.wait_ge(s_zero, 1)
            nc.scalar.activation(std[:, 0:1], eps[:, 0:1], ACT.Sqrt).then_inc(s_table, 1)
            act.wait_ge(s_table, 1)
            node_phase(0)
            act.wait_ge(s_keep, 4)
            act.wait_ge(s_setup, 1)
            for k in LAYERS:
                edge_phase(k)
                node_phase(k + 1)

        @block.vector
        def _(dve):
            steps = [0]

            def step(ins):
                steps[0] += 1
                ins.then_inc(s_masks, 1)
                dve.wait_ge(s_masks, steps[0])

            v = nc.vector
            v.memset(eps[:, :], EPS).then_inc(s_zero, 1)
            v.memset(ident[:, :], 0.0).then_inc(s_zero, 1)
            v.memset(zeros[:, :], 0.0).then_inc(s_zero, 1)
            v.memset(upper[:, :], 1.0).then_inc(s_zero, 1)
            v.memset(far_below[:, :], -FLT_MAX)
            v.memset(zeros_b[:, :], 0.0)
            v.memset(ends[:, 0:1], 0.0)
            v.memset(prev_t[D:D + 2, :, :], 1.0).then_inc(s_zero, 1)

            def setup():
                dve.wait_ge(s_consts, 3)
                dve.wait_ge(s_keep, 4)
                dve.wait_ge(s_dst, 16)
                v.tensor_copy(iota_b[:, :], iota_i[:, :])
                v.tensor_scalar(cont_add[:, :], cont_mul[:, :], 1.0, FLT_MAX, ALU.subtract, ALU.mult)
                step(v.scalar_tensor_tensor(out=work[:, 1:T], in0=keep_mul[:, 1:T], scalar=FAR,
                                            in1=slot_i[:, 1:T], op0=ALU.mult, op1=ALU.add))
                step(v.tensor_reduce(fix[:, :], work[:, 1:T], AX.X, ALU.min))
                step(v.tensor_scalar(whole[:, :], fix[:, :], FAR, None, ALU.is_ge))
                step(v.tensor_tensor(whole[:, :], whole[:, :], cont_mul[:, :], ALU.mult))
                v.tensor_scalar(whole_b[:, :], zeros[:, 0:D], whole[:, 0:1], None, ALU.add
                                ).then_inc(s_whole_bc, 1)
                step(v.tensor_scalar(fix[:, :], fix[:, :], float(T), 1.0, ALU.min, ALU.subtract))
                step(v.tensor_tensor(fix_row[:, :], fix[:, :], first_i[:, :], ALU.add))
                step(v.tensor_scalar(digits[:, 0, :], dst_sb[:, 1:T + 1], LO_MASK, None, ALU.bitwise_and))
                v.tensor_scalar(digits[:, 1, :], dst_sb[:, 1:T + 1], HI_SHIFT, None, ALU.logical_shift_right
                                ).then_inc(s_setup, 1)

            def layernorm(k, i, q, first, source, dest):
                b = i * NRING + q
                if not (first and q == 0):
                    dve.wait_ge(normed[k], b)
                for c in range(NB):
                    last = v.bn_stats(stats[:, c, :], source(i, q, c))
                last.then_inc(stat_step[k], 1)
                dve.wait_ge(stat_step[k], 2 * b + 1)
                dve.sem_inc(aggr_turn, 1)
                for c in range(NB):
                    last = v.bn_aggr(mean_var[:, c, :], stats[:, c, :])
                last.then_inc(var_ready[k], 1)
                dve.wait_ge(std_ready[k], b + 1)
                v.reciprocal(rstd[:, :], std[:, :]).then_inc(stat_step[k], 1)
                dve.wait_ge(stat_step[k], 2 * b + 2)
                if not first:
                    dve.wait_ge(feat_ready[k], b - NRING + 1)
                for c in range(NB):
                    last = v.tensor_scalar(dest[:, q, c, :], source(i, q, c), mean_var[:, c, 0:1],
                                           rstd[:, c:c + 1], ALU.subtract, ALU.mult)
                last.then_inc(normed[k], 1)

            def node_phase(k):
                def norm_x(i, q, first):
                    dve.wait_ge(s_x_first if first else s_x_rest, 16)
                    layernorm(0, i, q, first,
                              lambda i, q, c: resid[:, bass.ds(((i * NRING + q) * NB + c) * D, D)], act_t)

                def convolved(i, q, first):
                    b = i * NRING + q
                    dve.wait_ge(agg_loaded[k][q], (i + 1) * 16 * NB)
                    if k == 2 and not first:
                        dve.wait_ge(resid_kept[2], b - NRING + 1)
                        dve.wait_ge(normed[2], b - NRING + 1)
                    dve.wait_ge(root_done[k], b + 1)
                    v.tensor_tensor(flat(act_t[:, q, 0:HALF, :]), flat(agg[:, q, 0:HALF, :]),
                                    root_ps[q][0][:, 0:HALF * D], ALU.add)
                    v.tensor_tensor(flat(act_t[:, q, HALF:NB, :]), flat(agg[:, q, HALF:NB, :]),
                                    root_ps[q][1][:, 0:(NB - HALF) * D], ALU.add).then_inc(node_sum[k], 1)
                    dve.wait_ge(node_sum[k], b + 1)
                    if not first:
                        dve.wait_ge(transposed[1] if k == 1 else feat_ready[2], b - NRING + 1)
                    dest = feat if k == 1 else store
                    v.scalar_tensor_tensor(out=flat(dest[:, q]), in0=flat(act_t[:, q]), scalar=SLOPE,
                                           in1=flat(act_t[:, q]), op0=ALU.mult, op1=ALU.max
                                           ).then_inc(feat_ready[1] if k == 1 else conv_act, 1)

                def stage_rows(i, q, first):
                    dve.wait_ge(msg_done[k], i * NRING + q + 1)
                    if not first:
                        dve.wait_ge(stored[k][q], i * 16)
                    v.tensor_copy(flat(store[:, q, 0:HALF, :]), msg_ps[0][:, 0:HALF * D])
                    v.tensor_copy(flat(store[:, q, HALF:NB, :]), msg_ps[1][:, 0:(NB - HALF) * D]
                                  ).then_inc(store_ready[k], 1)

                def second_layer(i, first):
                    for q in range(NRING):
                        convolved(i, q, first)
                        b = i * NRING + q
                        dve.wait_ge(conv_act, b + 1)
                        v.tensor_tensor(flat(act_t[:, q]), flat(store[:, q]), resid[:, node_cols(i, q)],
                                        ALU.add).then_inc(node_act[2], 1)
                        dve.wait_ge(node_act[2], b + 1)
                        layernorm(2, i, q, first, lambda i, q, c: act_t[:, q, c, :], store)

                def output(i, first):
                    for q in range(NRING):
                        b = i * NRING + q
                        dve.wait_ge(msg_done[3], b + 1)
                        if not first:
                            dve.wait_ge(stored[3][q], i * 16)
                        parts = ((0, slice(0, HALF), HALF * D), (1, slice(HALF, NB), (NB - HALF) * D))
                        dve.wait_ge(root_kept, b + 1)
                        for part, tiles, cols in parts:
                            last = v.tensor_tensor(flat(act_t[:, q, tiles, :]), msg_ps[part][:, 0:cols],
                                                   flat(act_t[:, q, tiles, :]), ALU.add)
                        last.then_inc(out_sum, 1)
                        dve.wait_ge(out_sum, b + 1)
                        last = v.scalar_tensor_tensor(out=flat(store[:, q]), in0=flat(act_t[:, q]), scalar=0.0,
                                                      in1=resid[:, node_cols(i, q)], op0=ALU.max, op1=ALU.add)
                        last.then_inc(store_ready[3], 1)

                if k == 0:
                    node_loop(dve, lambda i, first: [norm_x(i, q, first) for q in range(NRING)])
                elif k == 1:
                    skewed_loop(dve, NITERS, NRING, convolved, stage_rows)
                else:
                    node_loop(dve, (second_layer, output)[k - 2])

            def edge_phase(k):
                join, op0, op1 = (ALU.mult, ALU.mult, ALU.add) if k == 2 else (ALU.add, ALU.add, ALU.max)
                v.memset(state_ring[:, RING - 1, SB - 1, :], 0.0).then_inc(state_init[k], 1)
                dve.wait_ge(state_init[k], 1)

                def body(i, first):
                    for r in range(RING):
                        b = i * RING + r
                        dve.wait_ge(keep_copied[k], b + 1)
                        if k == 0:
                            if not first:
                                dve.wait_ge(s_hist, b - RING + 1)
                            v.tensor_tensor(lo_hot[:, r], digit_ring[:, r, 0, :, None].to_broadcast([P, SB, P]),
                                            iota_b[:, None, :].to_broadcast([P, SB, P]), ALU.is_equal)
                            v.tensor_tensor(hi_hot[:, r], digit_ring[:, r, 1, :, None].to_broadcast([P, SB, HI]),
                                            iota_b[:, None, 0:HI].to_broadcast([P, SB, HI]), ALU.is_equal
                                            ).then_inc(s_hot, 1)
                        dve.wait_ge(term_ready[k], b + 1)
                        dve.wait_ge(gathered[k][r], (i + 1) * 16 * SB)
                        v.tensor_tensor(flat(rows_ring[:, r]), term[r][:, 0:BD], flat(rows_ring[:, r]), join
                                        ).then_inc(combined[k], 1)
                        dve.wait_ge(combined[k], b + 1)
                        if not first:
                            dve.wait_ge(dumped[k][r], i * 16)
                        for c in range(SB):
                            if c:
                                before_this = state_ring[:, r, c - 1, :]
                                dve.wait_ge(state_step[k], b * (SB - 1) + c)
                            else:
                                before_this = state_ring[:, (r - 1) % RING, SB - 1, :]
                                if not (first and r == 0):
                                    dve.wait_ge(scanned[k], b)
                            v.scalar_tensor_tensor(out=state_ring[:, r, c, :], in0=before_this,
                                                   scalar=keep_ring[:, r, c:c + 1], in1=rows_ring[:, r, c, :],
                                                   op0=op0, op1=op1
                                                   ).then_inc(state_step[k] if c < SB - 1 else scanned[k], 1)

                edge_loop(dve, body)

            def node_rows():
                seen = [0]

                def step(ins):
                    seen[0] += 1
                    ins.then_inc(s_pref, 1)
                    dve.wait_ge(s_pref, seen[0])

                dve.wait_ge(s_hist_end, 1)
                step(v.tensor_copy(count[:, :], count_ps[0:HI, 0:P]))
                v.tensor_reduce(total[:, :], count[:, :], AX.X, ALU.add).then_inc(s_total, 1)
                v.tensor_tensor_scan(prefix[:, :], count[:, :], zeros[0:HI, :], 0.0, ALU.add, ALU.add)
                v.tensor_scalar(empty[:, :], count[:, :], 0.0, None, ALU.is_equal)
                dve.wait_ge(s_before, 1)
                step(v.tensor_copy(before[:, :], before_ps[0:HI, 0:1]))
                step(v.tensor_scalar(prefix[:, :], prefix[:, :], before[:, 0:1], 1.0, ALU.add, ALU.subtract))
                step(v.tensor_scalar(node_row_f[:, :], prefix[:, :], -1.0, float(ZERO_ROW), ALU.mult, ALU.add))
                step(v.tensor_tensor(node_row_f[:, :], node_row_f[:, :], empty[:, :], ALU.mult))
                v.tensor_tensor(node_row_i[:, :], node_row_f[:, :], prefix[:, :], ALU.add
                                ).then_inc(s_noderow, 1)

            def stitch(k):
                op0, op1 = (ALU.mult, ALU.add) if k == 2 else (ALU.add, ALU.max)
                whole_row = whole_mul if k == 2 else whole_add
                if k == 0:
                    dve.wait_ge(s_whole_t, 1)
                    v.tensor_copy(whole_mul[:, :], whole_ps[0:D, 0:P])
                    step(v.tensor_scalar(whole_add[:, :], whole_ps[0:D, 0:P], 1.0, FLT_MAX,
                                         ALU.subtract, ALU.mult))
                dve.wait_ge(tail_t, k + 1)
                v.tensor_tensor_scan(ends[:, 1:P + 1], whole_row[:, :], tail_ps[0:D, 0:P], 0.0, op0, op1
                                     ).then_inc(ends_ready, 1)
                if k == 0:
                    node_rows()
                dve.wait_ge(ends_back, k + 1)
                dve.wait_ge(fix_loaded, 16 * (k + 1))
                cont = cont_mul if k == 2 else cont_add
                v.scalar_tensor_tensor(out=fix_vals[:, :], in0=shift_ps[:, 0:D], scalar=cont[:, 0:1],
                                       in1=fix_vals[:, :], op0=op0, op1=op1).then_inc(fix_ready, 1)

            node_phase(0)
            setup()
            for k in LAYERS:
                edge_phase(k)
                stitch(k)
                node_phase(k + 1)


def kernel(**inputs):
    import numpy as _np
    import concourse.bacc as _bacc
    from concourse import mybir as _mybir
    from concourse.bass_utils import run_bass_kernel_spmd as _run

    def get(name):
        return _np.asarray(inputs[name])

    def edge_attr(name, rows):
        a = get(name)
        w = a.shape[1]
        a = _np.pad(a, ((0, P * T - E), (0, rows - w)))
        return a.reshape(P, T, rows).transpose(2, 1, 0).reshape(rows, T * P)

    def rows(*parts):
        return _np.concatenate([_np.atleast_2d(a) for a in parts], axis=0)

    arrays = {
        "x": _np.pad(get("x"), ((0, NPAD - N), (0, 0))).reshape(P, NT * D),
        "src": _np.pad(get("src"), (0, P * T - E)).reshape(P, T),
        "dst": _np.pad(_np.pad(get("dst"), (1, 0), constant_values=-1), (0, P * T - E), constant_values=N),
        "ea32": edge_attr("edge_attr_32", DE0),
        "ea17": edge_attr("edge_attr_17", DE1P),
        "w1_msg": get("L0_gnn_W1_msg"),
        "w1_root": rows(get("L0_gnn_W1_root"), get("L0_gnn_b1")),
        "w1_edge": get("L0_gnn_W1_edge"),
        "w2_msg": get("L0_gnn_W2_msg"),
        "w2_root": rows(get("L0_gnn_W2_root"), get("L0_gnn_b2")),
        "w2_edge": get("L0_gnn_W2_edge"),
        "w3_h": _np.pad(get("L1_gnn_W1").T, ((0, DE1P - DE1), (0, 0))),
        "b3_h": get("L1_gnn_b1").reshape(D, 1),
        "w3_e": rows(get("L1_gnn_W2").T, get("L1_gnn_b2")),
        "w3_self": rows(get("L1_gnn_Ws").T, get("L1_gnn_bs"), get("L1_gnn_bn")),
        "w3_nbr": get("L1_gnn_Wn").T,
    }
    nc = _bacc.Bacc("TRN2", target_bir_lowering=False, num_devices=1)
    in_map, args = {}, []
    for name, a in arrays.items():
        a = _np.ascontiguousarray(a)
        in_map[f"in_{name}"] = a
        args.append(nc.dram_tensor(f"in_{name}", a.shape, _mybir.dt.from_np(a.dtype), kind="ExternalInput").ap())
    out = nc.dram_tensor("out_nodes", (P, NT * D), F32, kind="ExternalOutput").ap()
    gnn_program(nc, *args, out)
    r = _run(nc, [in_map], core_ids=[0])
    return r.results[0]["out_nodes"].reshape(NPAD, D)[:N]
```
